# Optimizing a Trainium2 kernel written in Bass

```python
import numpy as np
import jax
import jax.numpy as jnp

def _softmax(x, axis=-1):
    return jax.nn.softmax(x, axis=axis)

def _gelu(x):
    return jax.nn.gelu(x, approximate=True)

def _silu(x):
    return jax.nn.silu(x)

def _sigmoid(x):
    return jax.nn.sigmoid(x)

def _layernorm(x, axis=-1, eps=1e-05):
    m = jnp.mean(x, axis=axis, keepdims=True)
    v = jnp.var(x, axis=axis, keepdims=True)
    return (x - m) / jnp.sqrt(v + eps)

def _scatter_add(tgt, idx, src, axis=0):
    return tgt.at[idx].add(src)

def _segment_sum(src, seg, n):
    return jax.ops.segment_sum(src, seg, n)
kernel_name = 'mk_dlrm_tower_d1_rec_r8_0fa301'

def setup_inputs(seed: int=0):
    np.random.seed(seed)
    _w = jnp.asarray

    def _rec_inputs():
        import jax
        import jax.numpy as jnp
        _tk = jax.random.key(seed)
        ids = jnp.stack([jax.random.randint(jax.random.fold_in(_tk, 200 + f), (512,), 0, v, jnp.int32) for f, v in enumerate([1250, 125000, 1250, 1250, 1250, 1000, 1250, 1250, 1000, 12500, 12500, 1000, 1250, 1250, 1250, 12500, 12500, 1250, 1000, 1250, 1250, 12500, 1250, 1250, 1000, 12500])], axis=1)
        tbl_0 = 0.05 * jax.random.normal(jax.random.fold_in(_tk, 500 + 0), (1250, 128), jnp.float32)
        tbl_1 = 0.05 * jax.random.normal(jax.random.fold_in(_tk, 500 + 1), (125000, 128), jnp.float32)
        tbl_2 = 0.05 * jax.random.normal(jax.random.fold_in(_tk, 500 + 2), (1250, 128), jnp.float32)
        tbl_3 = 0.05 * jax.random.normal(jax.random.fold_in(_tk, 500 + 3), (1250, 128), jnp.float32)
        tbl_4 = 0.05 * jax.random.normal(jax.random.fold_in(_tk, 500 + 4), (1250, 128), jnp.float32)
        tbl_5 = 0.05 * jax.random.normal(jax.random.fold_in(_tk, 500 + 5), (1000, 128), jnp.float32)
        tbl_6 = 0.05 * jax.random.normal(jax.random.fold_in(_tk, 500 + 6), (1250, 128), jnp.float32)
        tbl_7 = 0.05 * jax.random.normal(jax.random.fold_in(_tk, 500 + 7), (1250, 128), jnp.float32)
        tbl_8 = 0.05 * jax.random.normal(jax.random.fold_in(_tk, 500 + 8), (1000, 128), jnp.float32)
        tbl_9 = 0.05 * jax.random.normal(jax.random.fold_in(_tk, 500 + 9), (12500, 128), jnp.float32)
        tbl_10 = 0.05 * jax.random.normal(jax.random.fold_in(_tk, 500 + 10), (12500, 128), jnp.float32)
        tbl_11 = 0.05 * jax.random.normal(jax.random.fold_in(_tk, 500 + 11), (1000, 128), jnp.float32)
        tbl_12 = 0.05 * jax.random.normal(jax.random.fold_in(_tk, 500 + 12), (1250, 128), jnp.float32)
        tbl_13 = 0.05 * jax.random.normal(jax.random.fold_in(_tk, 500 + 13), (1250, 128), jnp.float32)
        tbl_14 = 0.05 * jax.random.normal(jax.random.fold_in(_tk, 500 + 14), (1250, 128), jnp.float32)
        tbl_15 = 0.05 * jax.random.normal(jax.random.fold_in(_tk, 500 + 15), (12500, 128), jnp.float32)
        tbl_16 = 0.05 * jax.random.normal(jax.random.fold_in(_tk, 500 + 16), (12500, 128), jnp.float32)
        tbl_17 = 0.05 * jax.random.normal(jax.random.fold_in(_tk, 500 + 17), (1250, 128), jnp.float32)
        tbl_18 = 0.05 * jax.random.normal(jax.random.fold_in(_tk, 500 + 18), (1000, 128), jnp.float32)
        tbl_19 = 0.05 * jax.random.normal(jax.random.fold_in(_tk, 500 + 19), (1250, 128), jnp.float32)
        tbl_20 = 0.05 * jax.random.normal(jax.random.fold_in(_tk, 500 + 20), (1250, 128), jnp.float32)
        tbl_21 = 0.05 * jax.random.normal(jax.random.fold_in(_tk, 500 + 21), (12500, 128), jnp.float32)
        tbl_22 = 0.05 * jax.random.normal(jax.random.fold_in(_tk, 500 + 22), (1250, 128), jnp.float32)
        tbl_23 = 0.05 * jax.random.normal(jax.random.fold_in(_tk, 500 + 23), (1250, 128), jnp.float32)
        tbl_24 = 0.05 * jax.random.normal(jax.random.fold_in(_tk, 500 + 24), (1000, 128), jnp.float32)
        tbl_25 = 0.05 * jax.random.normal(jax.random.fold_in(_tk, 500 + 25), (12500, 128), jnp.float32)
        _rk = jax.random.fold_in(_tk, 7)
        r_dense_features = -0.000520686 + 1.00062 * jax.random.normal(jax.random.fold_in(_rk, 101), (512, 128), jnp.float32)
        W_top1 = 0.0405887 * jax.random.normal(jax.random.fold_in(_tk, 801), (607, 512), jnp.float32)
        W_top2 = 0.0441942 * jax.random.normal(jax.random.fold_in(_tk, 802), (512, 256), jnp.float32)
        W_top3 = 0.0625 * jax.random.normal(jax.random.fold_in(_tk, 803), (256, 1), jnp.float32)
        b_top1 = jnp.zeros((512,), jnp.float32)
        b_top2 = jnp.zeros((256,), jnp.float32)
        return (r_dense_features, ids, tbl_0, tbl_1, tbl_2, tbl_3, tbl_4, tbl_5, tbl_6, tbl_7, tbl_8, tbl_9, tbl_10, tbl_11, tbl_12, tbl_13, tbl_14, tbl_15, tbl_16, tbl_17, tbl_18, tbl_19, tbl_20, tbl_21, tbl_22, tbl_23, tbl_24, tbl_25, W_top1, b_top1, W_top2, b_top2, W_top3)
    r_dense_features, ids, tbl_0, tbl_1, tbl_2, tbl_3, tbl_4, tbl_5, tbl_6, tbl_7, tbl_8, tbl_9, tbl_10, tbl_11, tbl_12, tbl_13, tbl_14, tbl_15, tbl_16, tbl_17, tbl_18, tbl_19, tbl_20, tbl_21, tbl_22, tbl_23, tbl_24, tbl_25, W_top1, b_top1, W_top2, b_top2, W_top3 = _rec_inputs()

    def _L0_rec_setup():
        import jax, jax.numpy as jnp
        import numpy as np
        B, F, D = (2048, 26, 128)
        key = jax.random.key(seed)
        k1, k2 = jax.random.split(key)
        dense_features = jax.random.normal(k1, (B, D), dtype=jnp.float32)
        sparse_features = jax.random.normal(k2, (B, F, D), dtype=jnp.float32)
        return {'dense_features': dense_features, 'sparse_features': sparse_features}
    _L0_rec_all = _L0_rec_setup()
    _L0_rec_in = {k: v for k, v in _L0_rec_all.items() if k in ()}
    del _L0_rec_all
    return {'r_dense_features': r_dense_features, 'ids': ids, 'tbl_0': tbl_0, 'tbl_1': tbl_1, 'tbl_2': tbl_2, 'tbl_3': tbl_3, 'tbl_4': tbl_4, 'tbl_5': tbl_5, 'tbl_6': tbl_6, 'tbl_7': tbl_7, 'tbl_8': tbl_8, 'tbl_9': tbl_9, 'tbl_10': tbl_10, 'tbl_11': tbl_11, 'tbl_12': tbl_12, 'tbl_13': tbl_13, 'tbl_14': tbl_14, 'tbl_15': tbl_15, 'tbl_16': tbl_16, 'tbl_17': tbl_17, 'tbl_18': tbl_18, 'tbl_19': tbl_19, 'tbl_20': tbl_20, 'tbl_21': tbl_21, 'tbl_22': tbl_22, 'tbl_23': tbl_23, 'tbl_24': tbl_24, 'tbl_25': tbl_25, 'W_top1': W_top1, 'b_top1': b_top1, 'W_top2': W_top2, 'b_top2': b_top2, 'W_top3': W_top3}

def reference(r_dense_features, ids, tbl_0, tbl_1, tbl_2, tbl_3, tbl_4, tbl_5, tbl_6, tbl_7, tbl_8, tbl_9, tbl_10, tbl_11, tbl_12, tbl_13, tbl_14, tbl_15, tbl_16, tbl_17, tbl_18, tbl_19, tbl_20, tbl_21, tbl_22, tbl_23, tbl_24, tbl_25, W_top1, b_top1, W_top2, b_top2, W_top3):
    import jax
    import jax.numpy as jnp

    def _L0_rec_ref(dense_features, sparse_features):
        import jax, jax.numpy as jnp
        import numpy as np
        B, F, D = (2048, 26, 128)
        combined = jnp.concatenate([dense_features[:, None, :], sparse_features], axis=1)
        interactions = jnp.einsum('bfd,bgd->bfg', combined, combined)
        iu0, iu1 = np.triu_indices(F + 1, k=1)
        interactions_flat = interactions[:, iu0, iu1]
        return jnp.concatenate([dense_features, interactions_flat], axis=1)
    e = jnp.stack([tbl_0[ids[:, 0]], tbl_1[ids[:, 1]], tbl_2[ids[:, 2]], tbl_3[ids[:, 3]], tbl_4[ids[:, 4]], tbl_5[ids[:, 5]], tbl_6[ids[:, 6]], tbl_7[ids[:, 7]], tbl_8[ids[:, 8]], tbl_9[ids[:, 9]], tbl_10[ids[:, 10]], tbl_11[ids[:, 11]], tbl_12[ids[:, 12]], tbl_13[ids[:, 13]], tbl_14[ids[:, 14]], tbl_15[ids[:, 15]], tbl_16[ids[:, 16]], tbl_17[ids[:, 17]], tbl_18[ids[:, 18]], tbl_19[ids[:, 19]], tbl_20[ids[:, 20]], tbl_21[ids[:, 21]], tbl_22[ids[:, 22]], tbl_23[ids[:, 23]], tbl_24[ids[:, 24]], tbl_25[ids[:, 25]]], axis=1)
    z = _L0_rec_ref(r_dense_features, e)
    z = z.reshape(z.shape[0], -1)
    h = jnp.concatenate([z, r_dense_features], axis=1)
    h = jnp.maximum(h @ W_top1 + b_top1, 0.0)
    h = jnp.maximum(h @ W_top2 + b_top2, 0.0)
    y = h @ W_top3
    return y

_drawn_inputs = setup_inputs


def setup_inputs(seed=0):
    import zlib

    import numpy as np

    out = dict(_drawn_inputs(seed))
    spreads = {'b_top1': (0.0, 0.1), 'b_top2': (0.0, 0.1)}
    factors = {}
    for name, (base, spread) in spreads.items():
        noise = np.random.default_rng([zlib.crc32(name.encode()), seed]).standard_normal(out[name].shape)
        drawn = base * np.exp(spread * noise) if base else spread * noise
        out[name] = jnp.asarray(drawn.astype(out[name].dtype))
    for name, factor in factors.items():
        out[name] = (out[name] * factor).astype(out[name].dtype)
    return out
```

```python
import concourse.bass as bass
from concourse import mybir
from contextlib import ExitStack

BATCH, DIM = 512, 128
TABLES = 26
FEATURES = TABLES + 1
P = 128
TILES = BATCH // P
HIDDEN1, HIDDEN2 = 512, 256
H1C, H2C = HIDDEN1 // P, HIDDEN2 // P

SLOTS = 34
STAT0, STAT = 2, 32
MOVING = 29
REPEATED = SLOTS - FEATURES

CLASS_FEATURE = list(range(FEATURES))
GROUPS = [list(range(s, min(s + 4, FEATURES))) for s in range(0, FEATURES, 4)]

RECTS = [(2, 27, 1, 5, False), (2, 19, 6, 8, False), (21, 8, 6, 8, True)]
PAIRS = FEATURES * (FEATURES - 1) // 2
PAIR_TILES = [(at, min(P, PAIRS - at)) for at in range(0, PAIRS, P)]


def pair_rows():
    rows = []
    for c0, nc_, k0, nk, _ in RECTS:
        for c in range(c0, c0 + nc_):
            for k in range(k0, k0 + nk):
                i, j = sorted((CLASS_FEATURE[c % FEATURES], CLASS_FEATURE[(c + k) % FEATURES]))
                rows.append(DIM + i * FEATURES - i * (i + 1) // 2 + j - i - 1)
    return rows


def dlrm_tower_kernel(nc, dense, ids, tables, w_dense, w_pairs, b1, w2, b2, w3, out):
    f32, i32 = mybir.dt.float32, mybir.dt.int32
    ALU, ACT = mybir.AluOpType, mybir.ActivationFunctionType

    with ExitStack() as ctx:
        def sb(name, shape, dt=f32):
            return ctx.enter_context(nc.sbuf_tensor(name, shape, dt))

        def ps(name, shape):
            return ctx.enter_context(nc.psum_tensor(name, shape, f32))

        def sem(name):
            return ctx.enter_context(nc.semaphore(name))

        ids_sb = sb("ids_sb", [P, TILES, TABLES], i32)
        rows = sb("rows", [P, TILES, FEATURES, DIM])
        feat = sb("feat", [DIM, TILES, P, SLOTS])
        gram = sb("gram", [P, 2, MOVING, STAT])
        pairs = sb("pairs", [P, 2, len(PAIR_TILES) * P])
        pairs_t = sb("pairs_t", [P, 2, len(PAIR_TILES), P])
        ident = sb("ident", [P, P])
        w1d = sb("w1d", [P, 2, HIDDEN1])
        w1x = sb("w1x", [P, HIDDEN1])
        w1p = sb("w1p", [P, len(PAIR_TILES), HIDDEN1])
        w2_sb = sb("w2_sb", [P, H1C, HIDDEN2])
        w3_sb = sb("w3_sb", [P, H2C])
        b1_sb = sb("b1_sb", [P, H1C])
        b2_sb = sb("b2_sb", [P, H2C])
        h1 = sb("h1", [P, 2, H1C, P])
        h2 = sb("h2", [P, 2, H2C, P])
        y_sb = sb("y_sb", [1, BATCH])

        rows_ps = ps("rows_ps", [P, 2, 4, P])
        gram_ps = ps("gram_ps", [P, P // 4, STAT])
        pairs_ps = ps("pairs_ps", [P, 4, P])
        h1_ps = ps("h1_ps", [P, H1C, P])
        h2_ps = ps("h2_ps", [P, H1C, P])
        y_ps = ps("y_ps", [P, 512])

        ids_in, dense_in, w1_in, w2_in = sem("ids_in"), sem("dense_in"), sem("w1_in"), sem("w2_in")
        gathered = [[sem(f"gathered_{t}_{g}") for g in range(len(GROUPS))] for t in range(TILES)]
        ident_zero, ident_ready = sem("ident_zero"), sem("ident_ready")
        w1x_ready = sem("w1x_ready")
        rows_turned, feat_ready = sem("rows_turned"), sem("feat_ready")
        gram_done, gram_ready, packed = sem("gram_done"), sem("gram_ready"), sem("packed")
        pairs_turned, pairs_ready = sem("pairs_turned"), sem("pairs_ready")
        h1_done, h1_ready, h2_done, h2_ready = sem("h1_done"), sem("h1_ready"), sem("h2_done"), sem("h2_ready")
        y_done, y_ready, stored = sem("y_done"), sem("y_ready"), sem("stored")

        NG = len(GROUPS)
        block = ctx.enter_context(nc.Block())

        @block.sync
        def _(sp):
            sp.dma_start(ids_sb[:, :, :], ids.rearrange("(t p) f -> p t f", p=P)).then_inc(ids_in, 16)
            sp.dma_start(rows[:, :, 0, :], dense.rearrange("(t p) d -> p t d", p=P)).then_inc(dense_in, 16)
            sp.dma_start(w1d[:, :, :], w_dense.rearrange("(s p) n -> p s n", p=P)).then_inc(w1_in, 16)
            for n, (at, count) in enumerate(PAIR_TILES):
                sp.dma_start(w1p[0:count, n, :], w_pairs[at:at + count, :]).then_inc(w1_in, 16)
            sp.dma_start(b1_sb[:, :], b1).then_inc(w1_in, 16)
            sp.dma_start(w2_sb[:, :, :], w2.rearrange("(c p) n -> p c n", p=P)).then_inc(w2_in, 16)
            sp.dma_start(b2_sb[:, :], b2).then_inc(w2_in, 16)
            sp.dma_start(w3_sb[:, :], w3).then_inc(w2_in, 16)
            sp.wait_ge(y_ready, TILES)
            sp.dma_start(out.rearrange("b o -> o b"), y_sb[:, :]).then_inc(stored, 16)
            sp.wait_ge(stored, 16)

        @block.gpsimd
        def _(pool):
            pool.wait_ge(ident_zero, 1)
            nc.gpsimd.affine_select(out=ident[:, :], in_=ident[:, :], compare_op=ALU.not_equal, fill=1.0, base=0,
                                    pattern=[[-1, P]], channel_multiplier=1).then_inc(ident_ready, 1)
            pool.wait_ge(ids_in, 16)
            for t in range(TILES):
                for g, group in enumerate(GROUPS):
                    for c in group:
                        f = CLASS_FEATURE[c]
                        if f == 0:
                            continue
                        nc.gpsimd.indirect_dma_start(
                            rows[:, t, c, :], None, tables[f - 1],
                            bass.IndirectOffsetOnAxis(ap=ids_sb[:, t, f - 1:f], axis=0),
                        ).then_inc(gathered[t][g], 16)

        @block.tensor
        def _(pe):
            def turn_rows(t):
                for g, group in enumerate(GROUPS):
                    n = t * NG + g
                    if n == 0:
                        pe.wait_ge(dense_in, 16)
                    pe.wait_ge(gathered[t][g], 16 * sum(CLASS_FEATURE[c] > 0 for c in group))
                    if n >= 2:
                        pe.wait_ge(feat_ready, n - 1)
                    for s, c in enumerate(group):
                        last = nc.tensor.transpose(rows_ps[:, n % 2, s, :], rows[:, t, c, :], ident[:, :])
                    last.then_inc(rows_turned, 1)

            def gram_products(t):
                pe.wait_ge(feat_ready, (t + 1) * NG)
                if t >= 1:
                    pe.wait_ge(gram_ready, t)
                for i in range(P // 4):
                    for j in range(4):
                        b = 32 * j + i
                        last = nc.tensor.matmul(gram_ps[32 * j:32 * j + STAT, i, 0:MOVING],
                                                feat[:, t, b, STAT0:STAT0 + STAT], feat[:, t, b, 0:MOVING],
                                                start=True, stop=True)
                last.then_inc(gram_done, 1)

            def tower(t):
                u = t % 2
                pe.wait_ge(packed, t + 1)
                if t >= 1:
                    pe.wait_ge(pairs_ready, t)
                for n, (at, count) in enumerate(PAIR_TILES):
                    last = nc.tensor.transpose(pairs_ps[0:count, n, :], pairs[:, u, at:at + count], ident[:, :])
                last.then_inc(pairs_turned, 1)
                if t == 0:
                    pe.wait_ge(w1_in, 16 * (2 + len(PAIR_TILES)))
                    pe.wait_ge(w1x_ready, 1)
                pe.wait_ge(pairs_ready, t + 1)
                if t >= 1:
                    pe.wait_ge(h1_ready, t)
                for m in range(H1C):
                    nc.tensor.matmul(h1_ps[:, m, :], w1x[:, m * P:(m + 1) * P], feat[:, t, :, 0],
                                     start=True, stop=False)
                    for n, (at, count) in enumerate(PAIR_TILES):
                        last = nc.tensor.matmul(h1_ps[:, m, :], w1p[0:count, n, m * P:(m + 1) * P],
                                                pairs_t[0:count, u, n, :], start=False,
                                                stop=n == len(PAIR_TILES) - 1)
                last.then_inc(h1_done, 1)
                if t == 0:
                    pe.wait_ge(w2_in, 48)
                pe.wait_ge(h1_ready, t + 1)
                if t >= 1:
                    pe.wait_ge(h2_ready, t)
                for m in range(H2C):
                    for k in range(H1C):
                        last = nc.tensor.matmul(h2_ps[:, m, :], w2_sb[:, k, m * P:(m + 1) * P], h1[:, u, k, :],
                                                start=k == 0, stop=k == H1C - 1)
                last.then_inc(h2_done, 1)
                pe.wait_ge(h2_ready, t + 1)
                if t >= 1:
                    pe.wait_ge(y_ready, t)
                for k in range(H2C):
                    last = nc.tensor.matmul(y_ps[0:1, 0:P], w3_sb[:, k:k + 1], h2[:, u, k, :],
                                            start=k == 0, stop=k == H2C - 1)
                last.then_inc(y_done, 1)

            pe.wait_ge(ident_ready, 1)
            for t in range(TILES):
                turn_rows(t)
                gram_products(t)
                tower(t)

        @block.scalar
        def _(act):
            for t in range(TILES):
                for g, group in enumerate(GROUPS):
                    n = t * NG + g
                    act.wait_ge(rows_turned, n + 1)
                    c0, k = group[0], len(group)
                    again = min(c0 + k, REPEATED) - c0
                    if again > 0:
                        nc.scalar.copy(feat[:, t, :, FEATURES + c0:FEATURES + c0 + again].rearrange("d b s -> d s b"),
                                       rows_ps[:, n % 2, 0:again, :])
                    nc.scalar.copy(feat[:, t, :, c0:c0 + k].rearrange("d b s -> d s b"),
                                   rows_ps[:, n % 2, 0:k, :]).then_inc(feat_ready, 1)
                act.wait_ge(h1_done, t + 1)
                for m in range(H1C):
                    last = nc.scalar.activation(h1[:, t % 2, m, :], h1_ps[:, m, :], ACT.Relu, bias=b1_sb[:, m:m + 1])
                last.then_inc(h1_ready, 1)
                act.wait_ge(h2_done, t + 1)
                if t == 0:
                    act.wait_ge(w2_in, 48)
                for m in range(H2C):
                    last = nc.scalar.activation(h2[:, t % 2, m, :], h2_ps[:, m, :], ACT.Relu, bias=b2_sb[:, m:m + 1])
                last.then_inc(h2_ready, 1)
                act.wait_ge(y_done, t + 1)
                nc.scalar.copy(y_sb[0:1, t * P:(t + 1) * P], y_ps[0:1, 0:P]).then_inc(y_ready, 1)

        @block.vector
        def _(dve):
            nc.vector.memset(ident[:, :], 0.0).then_inc(ident_zero, 1)
            dve.wait_ge(w1_in, 16 * (2 + len(PAIR_TILES)))
            nc.vector.tensor_tensor(w1x[:, :], w1d[:, 0, :], w1d[:, 1, :], ALU.add).then_inc(w1x_ready, 1)
            for t in range(TILES):
                u = t % 2
                dve.wait_ge(gram_done, t + 1)
                nc.vector.transpose(gram[:, u, :, :], gram_ps[:, :, 0:MOVING].rearrange("p i c -> p c i")
                                    ).then_inc(gram_ready, 1)
                dve.wait_ge(gram_ready, t + 1)
                if t >= 2:
                    dve.wait_ge(pairs_turned, t - 1)
                flat = gram[:, u, :, :].rearrange("p c r -> p (c r)")
                at = 0
                for c0, cols, k0, dists, mirrored in RECTS:
                    if mirrored:
                        first = STAT * (c0 + k0 - FEATURES) + c0 - STAT0
                    else:
                        first = STAT * c0 + c0 + k0 - STAT0
                    v = flat[:, 0:cols * dists]
                    src = bass.AP(v.tensor, v.offset + first, [list(v.ap[0]), [STAT + 1, cols], [STAT if mirrored else 1, dists]])
                    last = nc.vector.tensor_copy(
                        pairs[:, u, at:at + cols * dists].rearrange("p (c k) -> p c k", c=cols), src)
                    at += cols * dists
                last.then_inc(packed, 1)
                dve.wait_ge(pairs_turned, t + 1)
                for n, (at, count) in enumerate(PAIR_TILES):
                    last = nc.vector.tensor_copy(pairs_t[0:count, u, n, :], pairs_ps[0:count, n, :])
                last.then_inc(pairs_ready, 1)


def kernel(**inputs):
    import numpy as np
    import concourse.bacc as bacc
    from concourse import mybir as mb
    from concourse.bass_utils import run_bass_kernel_spmd

    nc = bacc.Bacc("TRN2", target_bir_lowering=False, num_devices=1)
    arrays = {}

    def given(name, a):
        a = np.ascontiguousarray(a)
        arrays[name] = a
        return nc.dram_tensor(name, a.shape, mb.dt.from_np(a.dtype), kind="ExternalInput").ap()

    w1 = np.asarray(inputs["W_top1"])
    args = [
        given("dense", inputs["r_dense_features"]),
        given("ids", inputs["ids"]),
        [given(f"tbl_{n}", inputs[f"tbl_{n}"]) for n in range(TABLES)],
        given("w_dense", np.concatenate([w1[:DIM], w1[DIM + PAIRS:]])),
        given("w_pairs", w1[pair_rows()]),
        given("b1", np.asarray(inputs["b_top1"]).reshape(H1C, P).T),
        given("w2", inputs["W_top2"]),
        given("b2", np.asarray(inputs["b_top2"]).reshape(H2C, P).T),
        given("w3", np.asarray(inputs["W_top3"]).reshape(H2C, P).T),
    ]
    out = nc.dram_tensor("out", (BATCH, 1), mb.dt.float32, kind="ExternalOutput").ap()
    dlrm_tower_kernel(nc, *args, out)
    done = run_bass_kernel_spmd(nc, [arrays], core_ids=[0])
    return done.results[0]["out"]
```

```python
import concourse.bass as bass
from concourse import mybir
from contextlib import ExitStack

BATCH, DIM = 512, 128
TABLES = 26
FEATURES = TABLES + 1
P = 128
TILES = BATCH // P
HIDDEN1, HIDDEN2 = 512, 256
H1C, H2C = HIDDEN1 // P, HIDDEN2 // P

SLOTS = 34
STAT0, STAT = 2, 32
MOVING = 29
REPEATED = SLOTS - FEATURES

ROWS_OF = {5: 1000, 8: 1000, 11: 1000, 18: 1000, 24: 1000, 0: 1250, 2: 1250, 3: 1250}
ONE_HOT = list(ROWS_OF)
GATHERED = [n for n in range(TABLES) if n not in ONE_HOT]
CHUNK = 125
MOST_CHUNKS = max(ROWS_OF.values()) // CHUNK

CLASS_FEATURE = [0] + [1 + n for n in ONE_HOT + GATHERED]
GATHER0 = 1 + len(ONE_HOT)
GROUPS = [list(range(c, min(c + 4, FEATURES))) for c in range(GATHER0, FEATURES, 4)]
FILL = [GROUPS[0:2], GROUPS[2:3], GROUPS[3:4], GROUPS[4:]]
HOT_RING = 6

RECTS = [(2, 27, 1, 5, False), (2, 19, 6, 8, False), (21, 8, 6, 8, True)]
PAIRS = FEATURES * (FEATURES - 1) // 2
PAIR_TILES = [(at, min(P, PAIRS - at)) for at in range(0, PAIRS, P)]


def pair_rows():
    rows = []
    for c0, nc_, k0, nk, _ in RECTS:
        for c in range(c0, c0 + nc_):
            for k in range(k0, k0 + nk):
                i, j = sorted((CLASS_FEATURE[c % FEATURES], CLASS_FEATURE[(c + k) % FEATURES]))
                rows.append(DIM + i * FEATURES - i * (i + 1) // 2 + j - i - 1)
    return rows


def dlrm_tower_kernel(nc, dense, ids, hot_ids, tables, w_dense, w_pairs, b1, w2, b2, w3, out):
    f32, i32, f32r = mybir.dt.float32, mybir.dt.int32, mybir.dt.float32r
    ALU, ACT = mybir.AluOpType, mybir.ActivationFunctionType

    with ExitStack() as ctx:
        def sb(name, shape, dt=f32):
            return ctx.enter_context(nc.sbuf_tensor(name, shape, dt))

        def ps(name, shape):
            return ctx.enter_context(nc.psum_tensor(name, shape, f32))

        def sem(name):
            return ctx.enter_context(nc.semaphore(name))

        ids_sb = sb("ids_sb", [P, TILES, TABLES], i32)
        hot_ids_sb = sb("hot_ids_sb", [CHUNK, len(ONE_HOT), BATCH], i32)
        table = sb("table", [CHUNK, 3, MOST_CHUNKS, DIM])
        table_hi = sb("table_hi", [CHUNK, 2, MOST_CHUNKS, DIM], f32r)
        table_lo = sb("table_lo", [CHUNK, 2, MOST_CHUNKS, DIM], f32r)
        hot = sb("hot", [CHUNK, HOT_RING, BATCH], f32r)
        row_no_int = sb("row_no_int", [CHUNK, 2, MOST_CHUNKS], i32)
        row_no = sb("row_no", [CHUNK, 2, MOST_CHUNKS])
        dense_sb = sb("dense_sb", [P, TILES, DIM])
        rows = sb("rows", [P, 2, len(GATHERED), DIM])
        feat = sb("feat", [DIM, BATCH, SLOTS])
        gram = sb("gram", [P, MOVING, STAT])
        pairs = sb("pairs", [P, PAIRS])
        pairs_t = sb("pairs_t", [P, len(PAIR_TILES), P])
        ident = sb("ident", [P, P])
        w1d = sb("w1d", [P, 2, HIDDEN1])
        w1x = sb("w1x", [P, HIDDEN1])
        w1p = sb("w1p", [P, len(PAIR_TILES), HIDDEN1])
        w2_sb = sb("w2_sb", [P, H1C, HIDDEN2])
        w3_sb = sb("w3_sb", [P, H2C])
        b1_sb = sb("b1_sb", [P, H1C])
        b2_sb = sb("b2_sb", [P, H2C])
        h1 = sb("h1", [P, H1C, P])
        h2 = sb("h2", [P, H2C, P])
        y_sb = sb("y_sb", [1, BATCH])

        rows_ps = ps("rows_ps", [P, 2, 4, P])
        gram_ps = ps("gram_ps", [P, P // 4, STAT])
        pairs_ps = ps("pairs_ps", [P, 4, P])
        dense_ps = ps("dense_ps", [P, TILES, P])
        h2_ps = ps("h2_ps", [P, H2C, 4 * P])
        y_ps = h2_ps[0:1, 0, P:2 * P]
        h1_ps = [dense_ps[:, 0, :], gram_ps[:, 0:4, :].rearrange("p a b -> p (a b)"),
                 gram_ps[:, P // 8:P // 8 + 4, :].rearrange("p a b -> p (a b)"), pairs_ps[:, 0, :]]
        hot_ps = [h2_ps[:, 1, :], pairs_ps[:, :, :].rearrange("p a b -> p (a b)")]

        ids_in, dense_in, w1_in, w2_in = sem("ids_in"), sem("dense_in"), sem("w1_in"), sem("w2_in")
        hot_ids_in = [sem(f"hot_ids_in_{q}") for q in range(len(ONE_HOT))]
        table_in = [sem(f"table_in_{q}") for q in range(len(ONE_HOT))]
        gathered = [[sem(f"gathered_{t}_{g}") for g in range(len(GROUPS))] for t in range(TILES)]
        ident_zero, ident_ready = sem("ident_zero"), sem("ident_ready")
        row_no_int_ready, row_no_ready = sem("row_no_int_ready"), sem("row_no_ready")
        hi_ready, lo_ready, hot_ready, hot_used = sem("hi_ready"), sem("lo_ready"), sem("hot_ready"), sem("hot_used")
        dense_turned, hot_done, hot_feat_ready = sem("dense_turned"), sem("hot_done"), sem("hot_feat_ready")
        w1x_ready = sem("w1x_ready")
        rows_turned, feat_ready = sem("rows_turned"), sem("feat_ready")
        gram_done, gram_ready, packed = sem("gram_done"), sem("gram_ready"), sem("packed")
        pairs_turned, pairs_ready = sem("pairs_turned"), sem("pairs_ready")
        h1_done, h1_even, h1_odd = sem("h1_done"), sem("h1_even"), sem("h1_odd")
        h2_done, h2_even, h2_odd = sem("h2_done"), sem("h2_even"), sem("h2_odd")
        y_done, y_ready, stored = sem("y_done"), sem("y_ready"), sem("stored")

        NG = len(GROUPS)

        def chunks(q):
            return ROWS_OF[ONE_HOT[q]] // CHUNK

        def chunks_before(q):
            return sum(chunks(n) for n in range(q))

        block = ctx.enter_context(nc.Block())

        @block.sync
        def _(sp):
            sp.dma_start(ids_sb[:, :, :], ids.rearrange("(t p) f -> p t f", p=P)).then_inc(ids_in, 16)

            def load_table(q):
                rows_of = tables[ONE_HOT[q]].rearrange("(p k) d -> p k d", p=CHUNK)
                for lo, hi in ((0, 112), (112, CHUNK)):
                    sp.dma_start(table[lo:hi, q % 3, 0:chunks(q), :], rows_of[lo:hi]).then_inc(table_in[q], 16)
                sp.dma_start(hot_ids_sb[:, q, :], hot_ids[q:q + 1, :].partition_broadcast(CHUNK)
                             ).then_inc(hot_ids_in[q], 16)

            load_table(0)
            sp.dma_start(dense_sb[:, :, :], dense.rearrange("(t p) d -> p t d", p=P)).then_inc(dense_in, 16)
            load_table(1)
            load_table(2)
            sp.dma_start(w1d[:, :, :], w_dense.rearrange("(s p) n -> p s n", p=P)).then_inc(w1_in, 16)
            for n, (at, count) in enumerate(PAIR_TILES):
                sp.dma_start(w1p[0:count, n, :], w_pairs[at:at + count, :]).then_inc(w1_in, 16)
            sp.dma_start(b1_sb[:, :], b1).then_inc(w1_in, 16)
            sp.dma_start(w2_sb[:, :, :], w2.rearrange("(c p) n -> p c n", p=P)).then_inc(w2_in, 16)
            sp.dma_start(b2_sb[:, :], b2).then_inc(w2_in, 16)
            sp.dma_start(w3_sb[:, :], w3).then_inc(w2_in, 16)
            for q in range(3, len(ONE_HOT)):
                sp.wait_ge(lo_ready, q - 2)
                load_table(q)
            sp.wait_ge(y_ready, TILES)
            sp.dma_start(out.rearrange("b o -> o b"), y_sb[:, :]).then_inc(stored, 16)
            sp.wait_ge(stored, 16)

        @block.gpsimd
        def _(pool):
            for n, k in enumerate((8, 10)):
                last = nc.gpsimd.iota(row_no_int[:, n, 0:k], pattern=[[1, k]], base=0, channel_multiplier=k)
            last.then_inc(row_no_int_ready, 1)
            pool.wait_ge(ident_zero, 1)
            nc.gpsimd.affine_select(out=ident[:, :], in_=ident[:, :], compare_op=ALU.not_equal, fill=1.0, base=0,
                                    pattern=[[-1, P]], channel_multiplier=1).then_inc(ident_ready, 1)
            pool.wait_ge(ids_in, 16)
            for t in range(TILES):
                for g, group in enumerate(GROUPS):
                    if t >= 2:
                        pool.wait_ge(rows_turned, (t - 2) * NG + g + 1)
                    for c in group:
                        f = CLASS_FEATURE[c]
                        nc.gpsimd.indirect_dma_start(
                            rows[:, t % 2, c - GATHER0, :], None, tables[f - 1],
                            bass.IndirectOffsetOnAxis(ap=ids_sb[:, t, f - 1:f], axis=0),
                        ).then_inc(gathered[t][g], 16)

        @block.tensor
        def _(pe):
            def turn_dense():
                pe.wait_ge(ident_ready, 1)
                pe.wait_ge(dense_in, 16)
                for t in range(TILES):
                    last = nc.tensor.transpose(dense_ps[:, t, :], dense_sb[:, t, :], ident[:, :])
                last.then_inc(dense_turned, 1)

            def hot_products(q):
                if q >= 2:
                    pe.wait_ge(hot_feat_ready, q - 1)
                pe.wait_ge(hi_ready, q + 1)
                pe.wait_ge(lo_ready, q + 1)
                for k in range(chunks(q)):
                    n = chunks_before(q) + k
                    pe.wait_ge(hot_ready, n + 1)
                    nc.tensor.matmul(hot_ps[q % 2], table_hi[:, q % 2, k, :], hot[:, n % HOT_RING, :],
                                     start=k == 0, stop=False)
                    last = nc.tensor.matmul(hot_ps[q % 2], table_lo[:, q % 2, k, :], hot[:, n % HOT_RING, :],
                                            start=False, stop=k == chunks(q) - 1)
                    last.then_inc(hot_used, 1)

            def turn_rows(t, groups):
                for group in groups:
                    g = GROUPS.index(group)
                    n = t * NG + g
                    pe.wait_ge(gathered[t][g], 16 * len(group))
                    if n >= 2:
                        pe.wait_ge(feat_ready, n - 1)
                    for s, c in enumerate(group):
                        last = nc.tensor.transpose(rows_ps[:, n % 2, s, :], rows[:, t % 2, c - GATHER0, :], ident[:, :])
                    last.then_inc(rows_turned, 1)

            def gram_products(t):
                pe.wait_ge(feat_ready, (t + 1) * NG)
                if t == 0:
                    pe.wait_ge(hot_feat_ready, 1 + len(ONE_HOT))
                if t >= 1:
                    pe.wait_ge(gram_ready, t)
                for i in range(P // 4):
                    for j in range(4):
                        b = t * P + 32 * j + i
                        last = nc.tensor.matmul(gram_ps[32 * j:32 * j + STAT, i, 0:MOVING],
                                                feat[:, b, STAT0:STAT0 + STAT], feat[:, b, 0:MOVING],
                                                start=True, stop=True)
                last.then_inc(gram_done, 1)

            def turn_pairs(t):
                pe.wait_ge(packed, t + 1)
                if t >= 1:
                    pe.wait_ge(h1_odd, 2 * t)
                for n, (at, count) in enumerate(PAIR_TILES):
                    last = nc.tensor.transpose(pairs_ps[0:count, n, :], pairs[:, at:at + count], ident[:, :])
                last.then_inc(pairs_turned, 1)

            def layer1_dense(t):
                if t == 0:
                    pe.wait_ge(w1_in, 16 * (2 + len(PAIR_TILES)))
                    pe.wait_ge(w1x_ready, 1)
                    pe.wait_ge(hot_feat_ready, 1)
                pe.wait_ge(gram_ready, t + 1)
                for m in range(H1C - 1):
                    nc.tensor.matmul(h1_ps[m], w1x[:, m * P:(m + 1) * P], feat[:, t * P:(t + 1) * P, 0],
                                     start=True, stop=False)

            def layer1_pairs(t):
                pe.wait_ge(pairs_ready, t + 1)
                for m in range(H1C):
                    if m == H1C - 1:
                        nc.tensor.matmul(h1_ps[m], w1x[:, m * P:(m + 1) * P], feat[:, t * P:(t + 1) * P, 0],
                                         start=True, stop=False)
                    for n, (at, count) in enumerate(PAIR_TILES):
                        last = nc.tensor.matmul(h1_ps[m], w1p[0:count, n, m * P:(m + 1) * P],
                                                pairs_t[0:count, n, :], start=False,
                                                stop=n == len(PAIR_TILES) - 1)
                    last.then_inc(h1_done, 1)

            def layer2(t):
                if t == 0:
                    pe.wait_ge(w2_in, 48)
                if t >= 1:
                    pe.wait_ge(h2_even, t)
                    pe.wait_ge(h2_odd, t)
                    pe.wait_ge(y_ready, t)
                for k in range(H1C):
                    pe.wait_ge(h1_odd if k % 2 else h1_even, 2 * t + k // 2 + 1)
                    for m in range(H2C):
                        last = nc.tensor.matmul(h2_ps[:, m, 0:P], w2_sb[:, k, m * P:(m + 1) * P], h1[:, k, :],
                                                start=k == 0, stop=k == H1C - 1)
                last.then_inc(h2_done, 1)

            def layer3(t):
                for k in range(H2C):
                    pe.wait_ge(h2_odd if k % 2 else h2_even, t + 1)
                    last = nc.tensor.matmul(y_ps, w3_sb[:, k:k + 1], h2[:, k, :],
                                            start=k == 0, stop=k == H2C - 1)
                last.then_inc(y_done, 1)

            turn_dense()
            for q in range(len(ONE_HOT)):
                hot_products(q)
                turn_rows(0, GROUPS[q - 1:q] if q >= 1 else [])
            turn_rows(0, GROUPS[len(ONE_HOT) - 1:])
            for t in range(TILES):
                fill = FILL if t + 1 < TILES else [[]] * len(FILL)
                gram_products(t)
                turn_rows(t + 1, fill[0])
                turn_pairs(t)
                turn_rows(t + 1, fill[1])
                layer1_dense(t)
                layer1_pairs(t)
                turn_rows(t + 1, fill[2])
                layer2(t)
                turn_rows(t + 1, fill[3])
                layer3(t)

        @block.scalar
        def _(act):
            def split_hi(q):
                act.wait_ge(table_in[q], 32)
                if q >= 2:
                    act.wait_ge(hot_used, chunks_before(q - 1))
                    act.wait_ge(lo_ready, q - 1)
                nc.scalar.copy(table_hi[:, q % 2, 0:chunks(q), :], table[:, q % 3, 0:chunks(q), :]
                               ).then_inc(hi_ready, 1)

            def keep_class(c, src):
                if c < REPEATED:
                    nc.scalar.copy(feat[:, :, FEATURES + c], src)
                nc.scalar.copy(feat[:, :, c], src).then_inc(hot_feat_ready, 1)

            def keep_rows(t, groups):
                for group in groups:
                    n = t * NG + GROUPS.index(group)
                    act.wait_ge(rows_turned, n + 1)
                    c0, k = group[0], len(group)
                    own = feat[:, t * P:(t + 1) * P, :]
                    again = min(c0 + k, REPEATED) - c0
                    if again > 0:
                        nc.scalar.copy(own[:, :, FEATURES + c0:FEATURES + c0 + again].rearrange("d b s -> d s b"),
                                       rows_ps[:, n % 2, 0:again, :])
                    nc.scalar.copy(own[:, :, c0:c0 + k].rearrange("d b s -> d s b"),
                                   rows_ps[:, n % 2, 0:k, :]).then_inc(feat_ready, 1)

            split_hi(0)
            act.wait_ge(dense_turned, 1)
            keep_class(0, dense_ps[:, :, :].rearrange("d t b -> d (t b)"))
            split_hi(1)
            for q in range(len(ONE_HOT)):
                act.wait_ge(hot_used, chunks_before(q + 1))
                keep_class(1 + q, hot_ps[q % 2])
                if q + 2 < len(ONE_HOT):
                    split_hi(q + 2)
                keep_rows(0, GROUPS[q - 1:q] if q >= 1 else [])
            keep_rows(0, GROUPS[len(ONE_HOT) - 1:])
            for t in range(TILES):
                fill = FILL if t + 1 < TILES else [[]] * len(FILL)
                keep_rows(t + 1, fill[0])
                keep_rows(t + 1, fill[1])
                if t == 0:
                    act.wait_ge(w1_in, 16 * (2 + len(PAIR_TILES)))
                for m in range(0, H1C, 2):
                    act.wait_ge(h1_done, H1C * t + m + 1)
                    nc.scalar.activation(h1[:, m, :], h1_ps[m], ACT.Relu, bias=b1_sb[:, m:m + 1]
                                         ).then_inc(h1_even, 1)
                keep_rows(t + 1, fill[2])
                act.wait_ge(h2_done, t + 1)
                if t == 0:
                    act.wait_ge(w2_in, 48)
                nc.scalar.activation(h2[:, 0, :], h2_ps[:, 0, 0:P], ACT.Relu, bias=b2_sb[:, 0:1]).then_inc(h2_even, 1)
                keep_rows(t + 1, fill[3])
                act.wait_ge(y_done, t + 1)
                nc.scalar.copy(y_sb[0:1, t * P:(t + 1) * P], y_ps).then_inc(y_ready, 1)

        @block.vector
        def _(dve):
            def split_lo(q):
                dve.wait_ge(hi_ready, q + 1)
                if q >= 2:
                    dve.wait_ge(hot_used, chunks_before(q - 1))
                nc.vector.tensor_tensor(table_lo[:, q % 2, 0:chunks(q), :], table[:, q % 3, 0:chunks(q), :],
                                        table_hi[:, q % 2, 0:chunks(q), :], ALU.subtract).then_inc(lo_ready, 1)

            def make_hot(q):
                dve.wait_ge(hot_ids_in[q], 16)
                for k in range(chunks(q)):
                    n = chunks_before(q) + k
                    if n >= HOT_RING:
                        dve.wait_ge(hot_used, n - HOT_RING + 1)
                    nc.vector.tensor_scalar(hot[:, n % HOT_RING, :], hot_ids_sb[:, q, :],
                                            row_no[:, (8, 10).index(chunks(q)), k:k + 1], None, ALU.is_equal
                                            ).then_inc(hot_ready, 1)

            nc.vector.memset(ident[:, :], 0.0).then_inc(ident_zero, 1)
            dve.wait_ge(row_no_int_ready, 1)
            for n, k in enumerate((8, 10)):
                last = nc.vector.tensor_copy(row_no[:, n, 0:k], row_no_int[:, n, 0:k])
            last.then_inc(row_no_ready, 1)
            dve.wait_ge(row_no_ready, 1)
            for q in range(len(ONE_HOT)):
                split_lo(q)
                make_hot(q)
            dve.wait_ge(w1_in, 16 * (2 + len(PAIR_TILES)))
            nc.vector.tensor_tensor(w1x[:, :], w1d[:, 0, :], w1d[:, 1, :], ALU.add).then_inc(w1x_ready, 1)
            for t in range(TILES):
                dve.wait_ge(gram_done, t + 1)
                nc.vector.transpose(gram[:, :, :], gram_ps[:, :, 0:MOVING].rearrange("p i c -> p c i")
                                    ).then_inc(gram_ready, 1)
                dve.wait_ge(gram_ready, t + 1)
                if t >= 1:
                    dve.wait_ge(pairs_turned, t)
                at = 0
                for c0, cols, k0, dists, mirrored in RECTS:
                    if mirrored:
                        first = STAT * (c0 + k0 - FEATURES) + c0 - STAT0
                    else:
                        first = STAT * c0 + c0 + k0 - STAT0
                    v = gram[:, :, :]
                    src = bass.AP(v.tensor, v.offset + first,
                                  [list(v.ap[0]), [STAT + 1, cols], [STAT if mirrored else 1, dists]])
                    last = nc.vector.tensor_copy(
                        pairs[:, at:at + cols * dists].rearrange("p (c k) -> p c k", c=cols), src)
                    at += cols * dists
                last.then_inc(packed, 1)
                dve.wait_ge(pairs_turned, t + 1)
                for n, (at, count) in enumerate(PAIR_TILES):
                    last = nc.vector.tensor_copy(pairs_t[0:count, n, :], pairs_ps[0:count, n, :])
                last.then_inc(pairs_ready, 1)
                for m in range(1, H1C, 2):
                    dve.wait_ge(h1_done, H1C * t + m + 1)
                    nc.vector.tensor_scalar(h1[:, m, :], h1_ps[m], b1_sb[:, m:m + 1], 0.0, ALU.add, ALU.max
                                            ).then_inc(h1_odd, 1)
                if t == 0:
                    dve.wait_ge(w2_in, 48)
                dve.wait_ge(h2_done, t + 1)
                nc.vector.tensor_scalar(h2[:, 1, :], h2_ps[:, 1, 0:P], b2_sb[:, 1:2], 0.0, ALU.add, ALU.max
                                        ).then_inc(h2_odd, 1)


def kernel(**inputs):
    import numpy as np
    import concourse.bacc as bacc
    from concourse import mybir as mb
    from concourse.bass_utils import run_bass_kernel_spmd

    nc = bacc.Bacc("TRN2", target_bir_lowering=False, num_devices=1)
    arrays = {}

    def given(name, a):
        a = np.ascontiguousarray(a)
        arrays[name] = a
        return nc.dram_tensor(name, a.shape, mb.dt.from_np(a.dtype), kind="ExternalInput").ap()

    w1 = np.asarray(inputs["W_top1"])
    args = [
        given("dense", inputs["r_dense_features"]),
        given("ids", inputs["ids"]),
        given("hot_ids", np.asarray(inputs["ids"]).T[ONE_HOT]),
        [given(f"tbl_{n}", inputs[f"tbl_{n}"]) for n in range(TABLES)],
        given("w_dense", np.concatenate([w1[:DIM], w1[DIM + PAIRS:]])),
        given("w_pairs", w1[pair_rows()]),
        given("b1", np.asarray(inputs["b_top1"]).reshape(H1C, P).T),
        given("w2", inputs["W_top2"]),
        given("b2", np.asarray(inputs["b_top2"]).reshape(H2C, P).T),
        given("w3", np.asarray(inputs["W_top3"]).reshape(H2C, P).T),
    ]
    out = nc.dram_tensor("out", (BATCH, 1), mb.dt.float32, kind="ExternalOutput").ap()
    dlrm_tower_kernel(nc, *args, out)
    done = run_bass_kernel_spmd(nc, [arrays], core_ids=[0])
    return done.results[0]["out"]
```

```python
import concourse.bass as bass
from concourse import mybir
from contextlib import ExitStack

BATCH, DIM = 512, 128
TABLES = 26
FEATURES = TABLES + 1
P = 128
TILES = BATCH // P
HIDDEN1, HIDDEN2 = 512, 256
H1C, H2C = HIDDEN1 // P, HIDDEN2 // P

SLOTS = 34
STAT0, STAT = 2, 32
MOVING = 32
REPEATED = SLOTS - FEATURES

ONE_HOT = [5, 8, 11, 18, 24, 0, 2, 3]
LATE, LATE_FROM = 4, BATCH // 2
HOT = ONE_HOT + [LATE]
GATHERED = [n for n in range(TABLES) if n not in HOT] + [LATE]
CHUNK = 125

CLASS_FEATURE = [0] + [1 + n for n in ONE_HOT + GATHERED]
GATHER0 = 1 + len(ONE_HOT)
LATE_CLASS = FEATURES - 1
GROUPS = [list(range(c, min(c + 4, FEATURES))) for c in range(GATHER0, FEATURES, 4)]


def gathered_of(t, g):
    return [c for c in GROUPS[g] if c != LATE_CLASS or t * P < LATE_FROM]


FILL = [([], [1, 2], [3, 4])] + [([0, 1], [2, 3], [4])] * (TILES - 3) + [([0, 1], [2], [3, 4]), ([], [], [])]
FIRST_FILL = [[], [0], [1], [2], [3], [], [4], []]
ACT_CHUNKS = [1, 1, 1, 1, 1, 1, 2, 3, 1]
ACT_RING = 4
HOT_RING = 9

RECTS = [(2, 27, 1, 5, False), (2, 19, 6, 8, False), (21, 8, 6, 8, True)]
PAIRS = FEATURES * (FEATURES - 1) // 2
PAIR_TILES = 3
PAIR_ROWS = PAIRS // PAIR_TILES


def pair_rows():
    rows = []
    for c0, nc_, k0, nk, _ in RECTS:
        for c in range(c0, c0 + nc_):
            for k in range(k0, k0 + nk):
                i, j = sorted((CLASS_FEATURE[c % FEATURES], CLASS_FEATURE[(c + k) % FEATURES]))
                rows.append(DIM + i * FEATURES - i * (i + 1) // 2 + j - i - 1)
    return rows


def dlrm_tower_kernel(nc, dense, ids, hot_ids, tables, w_dense, w_pairs, b1, w2, b2, w3, out):
    f32, i32, f32r = mybir.dt.float32, mybir.dt.int32, mybir.dt.float32r
    ALU, ACT = mybir.AluOpType, mybir.ActivationFunctionType

    with ExitStack() as ctx:
        def sb(name, shape, dt=f32):
            return ctx.enter_context(nc.sbuf_tensor(name, shape, dt))

        def ps(name, shape):
            return ctx.enter_context(nc.psum_tensor(name, shape, f32))

        def sem(name):
            return ctx.enter_context(nc.semaphore(name))

        chunks_of = [tables[n].shape[0] // CHUNK for n in HOT]
        most_chunks = max(chunks_of)
        counts = sorted(set(chunks_of))

        ids_sb = sb("ids_sb", [P, TILES, TABLES], i32)
        hot_ids_sb = sb("hot_ids_sb", [CHUNK, len(HOT), BATCH], i32)
        table = sb("table", [CHUNK, 3, most_chunks, DIM])
        table_hi = sb("table_hi", [CHUNK, 3, most_chunks, DIM], f32r)
        table_lo = sb("table_lo", [CHUNK, 2, most_chunks, DIM], f32r)
        hot = sb("hot", [CHUNK, HOT_RING, BATCH], f32r)
        act_hot = sb("act_hot", [CHUNK, ACT_RING, BATCH], f32r)
        distance = sb("distance", [CHUNK, BATCH])
        row_no_int = sb("row_no_int", [CHUNK, len(counts), most_chunks], i32)
        row_no = sb("row_no", [CHUNK, len(counts), most_chunks])
        minus_row_no = sb("minus_row_no", [CHUNK, len(counts), most_chunks])
        dense_sb = sb("dense_sb", [P, TILES, DIM])
        rows = sb("rows", [P, 2, len(GATHERED), DIM])
        feat = sb("feat", [DIM, BATCH, SLOTS])
        gram = sb("gram", [P, MOVING, STAT])
        pairs = sb("pairs", [P, PAIRS])
        pairs_t = sb("pairs_t", [PAIR_ROWS, PAIR_TILES, P])
        ident = sb("ident", [P, P])
        w1d = sb("w1d", [P, 2, HIDDEN1])
        w1x = sb("w1x", [P, HIDDEN1])
        w1p = sb("w1p", [PAIR_ROWS, PAIR_TILES, HIDDEN1])
        w2_sb = sb("w2_sb", [P, H1C, HIDDEN2])
        w3_sb = sb("w3_sb", [P, H2C])
        b1_sb = sb("b1_sb", [P, H1C])
        b2_sb = sb("b2_sb", [P, H2C])
        h1 = sb("h1", [P, H1C, P])
        h2 = sb("h2", [P, H2C, P])
        y_sb = sb("y_sb", [1, BATCH])

        rows_ps = ps("rows_ps", [P, 2, 4, P])
        gram_ps = ps("gram_ps", [P, P // 4, STAT])
        pairs_ps = ps("pairs_ps", [P, 4, P])
        dense_ps = ps("dense_ps", [P, TILES, P])
        h2_ps = ps("h2_ps", [P, H2C, 4 * P])
        y_ps = h2_ps[0:1, 0, P:2 * P]
        h1_ps = [dense_ps[:, 0, :], gram_ps[:, 0:4, :].rearrange("p a b -> p (a b)"),
                 gram_ps[:, P // 8:P // 8 + 4, :].rearrange("p a b -> p (a b)"), pairs_ps[:, 0, :]]
        hot_ps = [h2_ps[:, 1, :], pairs_ps[:, :, :].rearrange("p a b -> p (a b)")]

        ids_in, dense_in, w1_in, w2_in = sem("ids_in"), sem("dense_in"), sem("w1_in"), sem("w2_in")
        hot_ids_in = [sem(f"hot_ids_in_{q}") for q in range(len(HOT))]
        table_in = [sem(f"table_in_{q}") for q in range(len(HOT))]
        first_table_rest_in = sem("first_table_rest_in")
        gathered = [[sem(f"gathered_{t}_{g}") for g in range(len(GROUPS))] for t in range(TILES)]
        ident_zero, ident_ready = sem("ident_zero"), sem("ident_ready")
        row_no_int_ready, row_no_ready = sem("row_no_int_ready"), sem("row_no_ready")
        hi_ready, lo_ready, hot_ready, hot_used = sem("hi_ready"), sem("lo_ready"), sem("hot_ready"), sem("hot_used")
        distance_ready, act_hot_ready = sem("distance_ready"), sem("act_hot_ready")
        dense_turned, hot_done, hot_feat_ready = sem("dense_turned"), sem("hot_done"), sem("hot_feat_ready")
        w1x_ready = sem("w1x_ready")
        rows_turned, feat_ready = sem("rows_turned"), sem("feat_ready")
        gram_done, gram_ready, packed = sem("gram_done"), sem("gram_ready"), sem("packed")
        pairs_turned, pairs_ready = sem("pairs_turned"), sem("pairs_ready")
        h1_done, h1_even, h1_odd = sem("h1_done"), sem("h1_even"), sem("h1_odd")
        h2_done, h2_even, h2_odd = sem("h2_done"), sem("h2_even"), sem("h2_odd")
        y_done, y_ready, stored = sem("y_done"), sem("y_ready"), sem("stored")

        NG = len(GROUPS)

        def chunks(q):
            return chunks_of[q]

        def samples(q):
            return slice(0 if q < len(ONE_HOT) else LATE_FROM, BATCH)

        def chunks_before(q):
            return sum(chunks(n) for n in range(q))

        def act_chunks_before(q):
            return sum(ACT_CHUNKS[:q])

        def dve_chunks(q):
            return chunks(q) - ACT_CHUNKS[q]

        def dve_chunks_before(q):
            return chunks_before(q) - act_chunks_before(q)

        used_dve = [chunks_before(q) + k + 1 for q in range(len(HOT)) for k in range(dve_chunks(q))]
        used_act = [chunks_before(q) + k + 1 for q in range(len(HOT)) for k in range(dve_chunks(q), chunks(q))]

        block = ctx.enter_context(nc.Block())

        @block.sync
        def _(sp):
            sp.dma_start(ids_sb[:, :, :], ids.rearrange("(t p) f -> p t f", p=P)).then_inc(ids_in, 16)

            def load_table(q, parts=1):
                rows_of = tables[HOT[q]].rearrange("(p k) d -> p k d", p=CHUNK)
                sp.dma_start(hot_ids_sb[:, q, :], hot_ids[q:q + 1, :].partition_broadcast(CHUNK)
                             ).then_inc(hot_ids_in[q], 16)
                for part in range(parts):
                    first, end = part * chunks(q) // parts, (part + 1) * chunks(q) // parts
                    for lo, hi in ((0, 112), (112, CHUNK)):
                        sp.dma_start(table[lo:hi, q % 3, first:end, :], rows_of[lo:hi, first:end, :]
                                     ).then_inc(table_in[q] if part == 0 else first_table_rest_in, 16)

            load_table(0, parts=2)
            load_table(1)
            sp.dma_start(dense_sb[:, :, :], dense.rearrange("(t p) d -> p t d", p=P)).then_inc(dense_in, 16)
            load_table(2)
            for q in range(3, len(HOT)):
                sp.wait_ge(lo_ready, q - 1)
                load_table(q)
            sp.dma_start(w1d[:, :, :], w_dense.rearrange("(s p) n -> p s n", p=P)).then_inc(w1_in, 16)
            sp.dma_start(w1p[:, :, :], w_pairs.rearrange("(n p) h -> p n h", p=PAIR_ROWS)).then_inc(w1_in, 16)
            sp.dma_start(b1_sb[:, :], b1).then_inc(w1_in, 16)
            sp.dma_start(w2_sb[:, :, :], w2.rearrange("(c p) n -> p c n", p=P)).then_inc(w2_in, 16)
            sp.dma_start(b2_sb[:, :], b2).then_inc(w2_in, 16)
            sp.dma_start(w3_sb[:, :], w3).then_inc(w2_in, 16)
            sp.wait_ge(y_ready, TILES)
            sp.dma_start(out.rearrange("b o -> o b"), y_sb[:, :]).then_inc(stored, 16)
            sp.wait_ge(stored, 16)

        @block.gpsimd
        def _(pool):
            for n, k in enumerate(counts):
                last = nc.gpsimd.iota(row_no_int[:, n, 0:k], pattern=[[1, k]], base=0, channel_multiplier=k)
            last.then_inc(row_no_int_ready, 1)
            pool.wait_ge(ident_zero, 1)
            nc.gpsimd.affine_select(out=ident[:, :], in_=ident[:, :], compare_op=ALU.not_equal, fill=1.0, base=0,
                                    pattern=[[-1, P]], channel_multiplier=1).then_inc(ident_ready, 1)
            pool.wait_ge(ids_in, 16)
            for t in range(TILES):
                for g in range(NG):
                    if t >= 2:
                        pool.wait_ge(rows_turned, (t - 2) * NG + g + 1)
                    for c in gathered_of(t, g):
                        f = CLASS_FEATURE[c]
                        nc.gpsimd.indirect_dma_start(
                            rows[:, t % 2, c - GATHER0, :], None, tables[f - 1],
                            bass.IndirectOffsetOnAxis(ap=ids_sb[:, t, f - 1:f], axis=0),
                        ).then_inc(gathered[t][g], 16)

        @block.tensor
        def _(pe):
            def turn_dense():
                pe.wait_ge(ident_ready, 1)
                pe.wait_ge(dense_in, 16)
                for t in range(TILES):
                    last = nc.tensor.transpose(dense_ps[:, t, :], dense_sb[:, t, :], ident[:, :])
                last.then_inc(dense_turned, 1)

            def hot_products(q):
                if q >= 2:
                    pe.wait_ge(hot_feat_ready, q)
                for k in range(chunks(q)):
                    if k == 0:
                        pe.wait_ge(lo_ready, q + 1 if q == 0 else q + 2)
                    elif q == 0 and k == chunks(0) // 2:
                        pe.wait_ge(lo_ready, 2)
                    if k < dve_chunks(q):
                        at = dve_chunks_before(q) + k
                        pe.wait_ge(hot_ready, at + 1)
                        moving = hot[:, at % HOT_RING, samples(q)]
                    else:
                        at = act_chunks_before(q) + k - dve_chunks(q)
                        pe.wait_ge(act_hot_ready, at + 1)
                        moving = act_hot[:, at % ACT_RING, samples(q)]
                    rows_t = hot_ps[q % 2][:, samples(q)]
                    nc.tensor.matmul(rows_t, table_hi[:, q % 3, k, :], moving, start=k == 0, stop=False)
                    nc.tensor.matmul(rows_t, table_lo[:, q % 2, k, :], moving,
                                     start=False, stop=k == chunks(q) - 1).then_inc(hot_used, 1)

            def turn_rows(t, groups):
                for g in groups:
                    n = t * NG + g
                    group = gathered_of(t, g)
                    pe.wait_ge(gathered[t][g], 16 * len(group))
                    if n >= 2:
                        pe.wait_ge(feat_ready, n - 1)
                    for s, c in enumerate(group):
                        last = nc.tensor.transpose(rows_ps[:, n % 2, s, :], rows[:, t % 2, c - GATHER0, :], ident[:, :])
                    last.then_inc(rows_turned, 1)

            def gram_products(t):
                pe.wait_ge(feat_ready, (t + 1) * NG)
                if t == 0:
                    pe.wait_ge(hot_feat_ready, 1 + len(ONE_HOT))
                if t >= 1:
                    pe.wait_ge(h1_even, 2 * t)
                    pe.wait_ge(h1_odd, 2 * t)
                for i in range(P // 4):
                    for j in range(4):
                        b = t * P + 32 * j + i
                        last = nc.tensor.matmul(gram_ps[32 * j:32 * j + STAT, i, 0:MOVING],
                                                feat[:, b, STAT0:STAT0 + STAT], feat[:, b, 0:MOVING],
                                                start=True, stop=True)
                last.then_inc(gram_done, 1)

            def turn_pairs(t):
                pe.wait_ge(packed, t + 1)
                if t == 0:
                    pe.wait_ge(hot_feat_ready, 2 + len(ONE_HOT))
                else:
                    pe.wait_ge(h1_odd, 2 * t)
                for n in range(PAIR_TILES):
                    last = nc.tensor.transpose(pairs_ps[0:PAIR_ROWS, n, :],
                                               pairs[:, n * PAIR_ROWS:(n + 1) * PAIR_ROWS], ident[:, :])
                last.then_inc(pairs_turned, 1)

            def layer1_dense(t):
                if t == 0:
                    pe.wait_ge(w1_in, 48)
                    pe.wait_ge(w1x_ready, 1)
                    pe.wait_ge(hot_feat_ready, 1)
                pe.wait_ge(gram_ready, t + 1)
                for m in range(H1C - 1):
                    nc.tensor.matmul(h1_ps[m], w1x[:, m * P:(m + 1) * P], feat[:, t * P:(t + 1) * P, 0],
                                     start=True, stop=False)

            def layer1_pairs(t):
                pe.wait_ge(pairs_ready, t + 1)
                for m in range(H1C):
                    if m == H1C - 1:
                        nc.tensor.matmul(h1_ps[m], w1x[:, m * P:(m + 1) * P], feat[:, t * P:(t + 1) * P, 0],
                                         start=True, stop=False)
                    for n in range(PAIR_TILES):
                        last = nc.tensor.matmul(h1_ps[m], w1p[:, n, m * P:(m + 1) * P], pairs_t[:, n, :],
                                                start=False, stop=n == PAIR_TILES - 1)
                    last.then_inc(h1_done, 1)

            def layer2(t, first=0, end=H1C):
                if t == 0:
                    pe.wait_ge(w2_in, 48)
                    pe.wait_ge(hot_feat_ready, 3 + len(ONE_HOT))
                if t >= 1 and first == 0:
                    pe.wait_ge(h2_even, t)
                    pe.wait_ge(h2_odd, t)
                    pe.wait_ge(y_ready, t)
                for k in range(first, end):
                    pe.wait_ge(h1_odd if k % 2 else h1_even, 2 * t + k // 2 + 1)
                    for m in range(H2C):
                        last = nc.tensor.matmul(h2_ps[:, m, 0:P], w2_sb[:, k, m * P:(m + 1) * P], h1[:, k, :],
                                                start=k == 0, stop=k == H1C - 1)
                if end == H1C:
                    last.then_inc(h2_done, 1)

            def layer3(t):
                for k in range(H2C):
                    pe.wait_ge(h2_odd if k % 2 else h2_even, t + 1)
                    last = nc.tensor.matmul(y_ps, w3_sb[:, k:k + 1], h2[:, k, :],
                                            start=k == 0, stop=k == H2C - 1)
                last.then_inc(y_done, 1)

            for q in range(len(ONE_HOT)):
                hot_products(q)
                if q == 0:
                    turn_dense()
                if q == len(ONE_HOT) - 1:
                    turn_rows(1, [0])
                turn_rows(0, FIRST_FILL[q])
            for t in range(TILES):
                before_pairs, after_pairs, after_layer1 = FILL[t]
                gram_products(t)
                if t == TILES - 1:
                    layer2(t - 1, H1C // 2, H1C)
                    layer1_dense(t)
                elif t >= 1:
                    layer3(t - 1)
                turn_rows(t + 1, before_pairs)
                if t == 0:
                    hot_products(len(HOT) - 1)
                if t < TILES - 1:
                    layer1_dense(t)
                turn_pairs(t)
                if t == TILES - 1:
                    layer3(t - 1)
                turn_rows(t + 1, after_pairs)
                layer1_pairs(t)
                turn_rows(t + 1, after_layer1)
                layer2(t, 0, H1C // 2 if t == TILES - 2 else H1C)
            layer3(TILES - 1)

        @block.scalar
        def _(act):
            def split_hi(q, part=0, parts=1):
                first, end = part * chunks(q) // parts, (part + 1) * chunks(q) // parts
                act.wait_ge(table_in[q] if part == 0 else first_table_rest_in, 32)
                if q >= 3:
                    act.wait_ge(hot_used, chunks_before(q - 2))
                nc.scalar.copy(table_hi[:, q % 3, first:end, :], table[:, q % 3, first:end, :]
                               ).then_inc(hi_ready, 1)

            def make_hot(q):
                act.wait_ge(hot_ids_in[q], 16)
                if q == 0:
                    act.wait_ge(row_no_ready, 1)
                for k in range(dve_chunks(q), chunks(q)):
                    n = act_chunks_before(q) + k - dve_chunks(q)
                    if n >= 1:
                        act.wait_ge(act_hot_ready, n)
                    nc.scalar.activation(distance[:, :], hot_ids_sb[:, q, :], ACT.Abs,
                                         bias=minus_row_no[:, counts.index(chunks(q)), k:k + 1]
                                         ).then_inc(distance_ready, 1)
                    act.wait_ge(distance_ready, n + 1)
                    if n >= ACT_RING:
                        act.wait_ge(hot_used, used_act[n - ACT_RING])
                    nc.scalar.activation(act_hot[:, n % ACT_RING, :], distance[:, :], ACT.Relu, bias=1.0, scale=-1.0
                                         ).then_inc(act_hot_ready, 1)

            def keep_class(c, src, lo, hi):
                if c < REPEATED:
                    nc.scalar.copy(feat[:, lo:hi, FEATURES + c], src[:, lo:hi])
                nc.scalar.copy(feat[:, lo:hi, c], src[:, lo:hi]).then_inc(hot_feat_ready, 1)

            def keep_rows(t, groups):
                for g in groups:
                    n = t * NG + g
                    group = gathered_of(t, g)
                    act.wait_ge(rows_turned, n + 1)
                    c0, k = group[0], len(group)
                    own = feat[:, t * P:(t + 1) * P, :]
                    again = min(c0 + k, REPEATED) - c0
                    if again > 0:
                        nc.scalar.copy(own[:, :, FEATURES + c0:FEATURES + c0 + again].rearrange("d b s -> d s b"),
                                       rows_ps[:, n % 2, 0:again, :])
                    nc.scalar.copy(own[:, :, c0:c0 + k].rearrange("d b s -> d s b"),
                                   rows_ps[:, n % 2, 0:k, :]).then_inc(feat_ready, 1)

            def relu1_even(t):
                if t == 0:
                    act.wait_ge(w1_in, 48)
                for m in range(0, H1C, 2):
                    act.wait_ge(h1_done, H1C * t + m + 1)
                    nc.scalar.activation(h1[:, m, :], h1_ps[m], ACT.Relu, bias=b1_sb[:, m:m + 1]).then_inc(h1_even, 1)

            def relu2_even(t):
                if t == 0:
                    act.wait_ge(w2_in, 48)
                act.wait_ge(h2_done, t + 1)
                nc.scalar.activation(h2[:, 0, :], h2_ps[:, 0, 0:P], ACT.Relu, bias=b2_sb[:, 0:1]).then_inc(h2_even, 1)

            def keep_y(t):
                act.wait_ge(y_done, t + 1)
                nc.scalar.copy(y_sb[0:1, t * P:(t + 1) * P], y_ps).then_inc(y_ready, 1)

            split_hi(0, 0, 2)
            split_hi(0, 1, 2)
            make_hot(0)
            split_hi(1)
            for q in range(len(ONE_HOT)):
                if q + 1 < len(ONE_HOT):
                    make_hot(q + 1)
                if q + 2 < len(HOT):
                    split_hi(q + 2)
                act.wait_ge(hot_used, chunks_before(q + 1))
                if q == 0:
                    act.wait_ge(dense_turned, 1)
                    keep_class(0, dense_ps[:, :, :].rearrange("d t b -> d (t b)"), 0, BATCH)
                if q + 1 < len(ONE_HOT):
                    keep_class(1 + q, hot_ps[q % 2], 0, BATCH)
                else:
                    keep_class(1 + q, hot_ps[q % 2], 0, P)
                    keep_rows(1, [0])
                    keep_class(1 + q, hot_ps[q % 2], P, BATCH)
                keep_rows(0, FIRST_FILL[q])
            for t in range(TILES):
                before_pairs, after_pairs, after_layer1 = FILL[t]
                if t == TILES - 1:
                    relu2_even(t - 1)
                if t >= 1:
                    keep_y(t - 1)
                keep_rows(t + 1, before_pairs)
                if t == 0:
                    q = len(HOT) - 1
                    make_hot(q)
                    act.wait_ge(hot_used, chunks_before(q + 1))
                    keep_class(LATE_CLASS, hot_ps[q % 2], LATE_FROM, BATCH)
                keep_rows(t + 1, after_pairs)
                relu1_even(t)
                keep_rows(t + 1, after_layer1)
                if t != TILES - 2:
                    relu2_even(t)
            keep_y(TILES - 1)

        @block.vector
        def _(dve):
            def split_lo(q, part=0, parts=1):
                first, end = part * chunks(q) // parts, (part + 1) * chunks(q) // parts
                dve.wait_ge(hi_ready, q + 2 if q >= 1 else part + 1)
                if q >= 2:
                    dve.wait_ge(hot_used, chunks_before(q - 1))
                nc.vector.tensor_tensor(table_lo[:, q % 2, first:end, :], table[:, q % 3, first:end, :],
                                        table_hi[:, q % 3, first:end, :], ALU.subtract).then_inc(lo_ready, 1)

            def make_hot(q, first, end):
                if first == 0:
                    dve.wait_ge(hot_ids_in[q], 16)
                for k in range(first, end):
                    n = dve_chunks_before(q) + k
                    if n >= HOT_RING:
                        dve.wait_ge(hot_used, used_dve[n - HOT_RING])
                    nc.vector.tensor_scalar(hot[:, n % HOT_RING, samples(q)], hot_ids_sb[:, q, samples(q)],
                                            row_no[:, counts.index(chunks(q)), k:k + 1], None, ALU.is_equal
                                            ).then_inc(hot_ready, 1)

            def relu2_odd(t):
                if t == 0:
                    dve.wait_ge(w2_in, 48)
                dve.wait_ge(h2_done, t + 1)
                nc.vector.tensor_scalar(h2[:, 1, :], h2_ps[:, 1, 0:P], b2_sb[:, 1:2], 0.0, ALU.add, ALU.max
                                        ).then_inc(h2_odd, 1)

            nc.vector.memset(ident[:, :], 0.0).then_inc(ident_zero, 1)
            dve.wait_ge(row_no_int_ready, 1)
            for n, k in enumerate(counts):
                nc.vector.tensor_copy(row_no[:, n, 0:k], row_no_int[:, n, 0:k])
                last = nc.vector.tensor_scalar(minus_row_no[:, n, 0:k], row_no_int[:, n, 0:k], -1.0, None, ALU.mult)
            last.then_inc(row_no_ready, 1)
            dve.wait_ge(row_no_ready, 1)
            make_hot(0, 0, 1)
            split_lo(0, 0, 2)
            make_hot(0, 1, 4)
            split_lo(0, 1, 2)
            make_hot(0, 4, dve_chunks(0))
            for q in range(1, len(HOT)):
                if q == len(HOT) - 1:
                    dve.wait_ge(w1_in, 48)
                    nc.vector.tensor_tensor(w1x[:, :], w1d[:, 0, :], w1d[:, 1, :], ALU.add).then_inc(w1x_ready, 1)
                split_lo(q)
                make_hot(q, 0, dve_chunks(q))
            for t in range(TILES):
                dve.wait_ge(gram_done, t + 1)
                nc.vector.transpose(gram[:, :, :], gram_ps[:, :, 0:MOVING].rearrange("p i c -> p c i")
                                    ).then_inc(gram_ready, 1)
                dve.wait_ge(gram_ready, t + 1)
                if t >= 1:
                    dve.wait_ge(pairs_turned, t)
                at = 0
                for c0, cols, k0, dists, mirrored in RECTS:
                    if mirrored:
                        first = STAT * (c0 + k0 - FEATURES) + c0 - STAT0
                    else:
                        first = STAT * c0 + c0 + k0 - STAT0
                    v = gram[:, :, :]
                    src = bass.AP(v.tensor, v.offset + first,
                                  [list(v.ap[0]), [STAT + 1, cols], [STAT if mirrored else 1, dists]])
                    last = nc.vector.tensor_copy(
                        pairs[:, at:at + cols * dists].rearrange("p (c k) -> p c k", c=cols), src)
                    at += cols * dists
                last.then_inc(packed, 1)
                if t == TILES - 1:
                    relu2_odd(t - 1)
                dve.wait_ge(pairs_turned, t + 1)
                nc.vector.tensor_copy(pairs_t[:, :, :], pairs_ps[0:PAIR_ROWS, 0:PAIR_TILES, :]).then_inc(pairs_ready, 1)
                for m in range(1, H1C, 2):
                    dve.wait_ge(h1_done, H1C * t + m + 1)
                    nc.vector.tensor_scalar(h1[:, m, :], h1_ps[m], b1_sb[:, m:m + 1], 0.0, ALU.add, ALU.max
                                            ).then_inc(h1_odd, 1)
                if t != TILES - 2:
                    relu2_odd(t)


def kernel(**inputs):
    import numpy as np
    import concourse.bacc as bacc
    from concourse import mybir as mb
    from concourse.bass_utils import run_bass_kernel_spmd

    nc = bacc.Bacc("TRN2", target_bir_lowering=False, num_devices=1)
    arrays = {}

    def given(name, a):
        a = np.ascontiguousarray(a)
        arrays[name] = a
        return nc.dram_tensor(name, a.shape, mb.dt.from_np(a.dtype), kind="ExternalInput").ap()

    w1 = np.asarray(inputs["W_top1"])
    args = [
        given("dense", inputs["r_dense_features"]),
        given("ids", inputs["ids"]),
        given("hot_ids", np.asarray(inputs["ids"]).T[HOT]),
        [given(f"tbl_{n}", inputs[f"tbl_{n}"]) for n in range(TABLES)],
        given("w_dense", np.concatenate([w1[:DIM], w1[DIM + PAIRS:]])),
        given("w_pairs", w1[pair_rows()]),
        given("b1", np.asarray(inputs["b_top1"]).reshape(H1C, P).T),
        given("w2", inputs["W_top2"]),
        given("b2", np.asarray(inputs["b_top2"]).reshape(H2C, P).T),
        given("w3", np.asarray(inputs["W_top3"]).reshape(H2C, P).T),
    ]
    out = nc.dram_tensor("out", (BATCH, 1), mb.dt.float32, kind="ExternalOutput").ap()
    dlrm_tower_kernel(nc, *args, out)
    done = run_bass_kernel_spmd(nc, [arrays], core_ids=[0])
    return done.results[0]["out"]
```
